# Optimizing a Trainium2 kernel written in Bass

```python
import numpy as np
import jax
import jax.numpy as jnp

def _softmax(x, axis=-1):
    return jax.nn.softmax(x, axis=axis)

def _gelu(x):
    return jax.nn.gelu(x, approximate=True)

def _silu(x):
    return jax.nn.silu(x)

def _sigmoid(x):
    return jax.nn.sigmoid(x)

def _layernorm(x, axis=-1, eps=1e-05):
    m = jnp.mean(x, axis=axis, keepdims=True)
    v = jnp.var(x, axis=axis, keepdims=True)
    return (x - m) / jnp.sqrt(v + eps)

def _scatter_add(tgt, idx, src, axis=0):
    return tgt.at[idx].add(src)

def _segment_sum(src, seg, n):
    return jax.ops.segment_sum(src, seg, n)
kernel_name = 'mk_gnn_ffn_d1_gnn_r8_e8de7c'

def setup_inputs(seed: int=0):
    np.random.seed(seed)
    _w = jnp.asarray

    def _rec_inputs():
        import jax
        import jax.numpy as jnp
        _gk = jax.random.key(seed)
        x = -0.0003713 + 1 * jax.random.normal(jax.random.fold_in(_gk, 1), (6250, 256), jnp.float32)
        src = jax.random.randint(jax.random.fold_in(_gk, 2), (100000,), 0, 6250, jnp.int32)
        dst = jnp.minimum((6250 * jax.random.uniform(jax.random.fold_in(_gk, 3), (100000,)) ** 2.0).astype(jnp.int32), 49999)
        _o = jnp.argsort(dst, stable=True)
        src = src[_o]
        dst = dst[_o]
        edge_type_8 = jax.random.randint(jax.random.fold_in(_gk, 12), (100000,), 0, 8, jnp.int32)
        return (x, src, dst, edge_type_8)
    x, src, dst, edge_type_8 = _rec_inputs()

    def _L0_gnn_setup():
        import jax, jax.numpy as jnp
        import numpy as np
        N, E, D, R, L = (6250, 31250, 256, 8, 3)
        key = jax.random.key(seed)
        k = jax.random.split(key, 7)
        scale = 1.0 / np.sqrt(D)
        x = jax.random.normal(k[0], (N, D), dtype=jnp.float32)
        edge_index = jax.random.randint(k[1], (2, E), 0, N, dtype=jnp.int64)
        edge_type = jax.random.randint(k[2], (E,), 0, R, dtype=jnp.int64)
        W_rel = jax.random.normal(k[3], (L, R, D, D), dtype=jnp.float32) * scale
        W_root = jax.random.normal(k[4], (L, D, D), dtype=jnp.float32) * scale
        bias = jax.random.normal(k[5], (L, D), dtype=jnp.float32) * 0.02
        return {'x': x, 'edge_index': edge_index, 'edge_type': edge_type, 'W_rel': W_rel, 'W_root': W_root, 'bias': bias}
    _L0_gnn_all = _L0_gnn_setup()
    _L0_gnn_in = {k: v for k, v in _L0_gnn_all.items() if k in ('W_rel', 'W_root', 'bias')}
    del _L0_gnn_all

    def _L0_ffn_setup():
        import math
        import jax, jax.numpy as jnp
        import numpy as np
        CAPACITY_FACTOR = 1.25
        key = jax.random.key(seed)
        ks = jax.random.split(key, 5)
        B, L, D, F, E = (8, 1024, 256, 1024, 8)
        h = jax.random.normal(ks[0], (B, L, D), dtype=jnp.float32)
        gate_w = jax.random.normal(ks[1], (D, E), dtype=jnp.float32) * 0.02
        gate_b = jnp.zeros((E,), dtype=jnp.float32)
        w1 = jax.random.normal(ks[2], (E, D, F), dtype=jnp.float32) * (1.0 / math.sqrt(D))
        b1 = jnp.zeros((E, F), dtype=jnp.float32)
        w2 = jax.random.normal(ks[3], (E, F, D), dtype=jnp.float32) * (1.0 / math.sqrt(F))
        b2 = jnp.zeros((E, D), dtype=jnp.float32)
        return {'h': h, 'gate_w': gate_w, 'gate_b': gate_b, 'w1': w1, 'b1': b1, 'w2': w2, 'b2': b2}
    _L0_ffn_all = _L0_ffn_setup()
    _L0_ffn_in = {k: v for k, v in _L0_ffn_all.items() if k in ('gate_w', 'gate_b', 'w1', 'b1', 'w2', 'b2')}
    del _L0_ffn_all
    return {'x': x, 'src': src, 'dst': dst, 'edge_type_8': edge_type_8, 'L0_gnn_W_rel': _L0_gnn_in['W_rel'], 'L0_gnn_W_root': _L0_gnn_in['W_root'], 'L0_gnn_bias': _L0_gnn_in['bias'], 'L0_ffn_gate_w': _L0_ffn_in['gate_w'], 'L0_ffn_gate_b': _L0_ffn_in['gate_b'], 'L0_ffn_w1': _L0_ffn_in['w1'], 'L0_ffn_b1': _L0_ffn_in['b1'], 'L0_ffn_w2': _L0_ffn_in['w2'], 'L0_ffn_b2': _L0_ffn_in['b2']}

def reference(x, src, dst, edge_type_8, L0_gnn_W_rel, L0_gnn_W_root, L0_gnn_bias, L0_ffn_gate_w, L0_ffn_gate_b, L0_ffn_w1, L0_ffn_b1, L0_ffn_w2, L0_ffn_b2):
    import jax
    import jax.numpy as jnp

    def _L0_gnn_ref(x, edge_index, edge_type, W_rel, W_root, bias):
        import jax, jax.numpy as jnp
        import numpy as np
        N, E, D, R, L = (6250, 31250, 256, 8, 3)
        src, dst = (edge_index[0], edge_index[1])
        n_layers = W_rel.shape[0]
        for l in range(n_layers):
            xr = jnp.einsum('nd,rde->rne', x, W_rel[l])
            msg = xr[edge_type, src]
            agg = jax.ops.segment_sum(msg, dst, num_segments=x.shape[0])
            x = jax.nn.relu(agg + x @ W_root[l] + bias[l])
        return x

    def _L0_ffn_ref(h, gate_w, gate_b, w1, b1, w2, b2):
        import math
        import jax, jax.numpy as jnp
        import numpy as np
        CAPACITY_FACTOR = 1.25
        B, L, D = h.shape
        E = gate_w.shape[1]
        T = B * L
        C = max(1, math.ceil(CAPACITY_FACTOR * T / E))
        x = h.reshape(T, D)
        logits = x @ gate_w + gate_b
        probs = jax.nn.softmax(logits, axis=-1)
        idx = jnp.argmax(probs, axis=-1)
        prb = jnp.take_along_axis(probs, idx[:, None], axis=1)[:, 0]
        one_hot = jax.nn.one_hot(idx, E, dtype=jnp.float32)
        pos = (jnp.cumsum(one_hot, axis=0) * one_hot).sum(-1).astype(jnp.int32) - 1
        kept = pos < C
        pos_safe = jnp.where(kept, pos, C)
        buf = jnp.zeros((E, C, D), dtype=h.dtype).at[idx, pos_safe].set(x, mode='drop')
        hmid = jax.nn.relu(jnp.einsum('ecd,edf->ecf', buf, w1) + b1[:, None, :])
        ybuf = jnp.einsum('ecf,efd->ecd', hmid, w2) + b2[:, None, :]
        pos_g = jnp.minimum(pos, C - 1)
        y_tok = ybuf[idx, pos_g] * (prb * kept)[:, None]
        y = y_tok.reshape(B, L, D)
        y = jnp.nan_to_num(y, nan=0.0, posinf=10000.0, neginf=-10000.0)
        return y
    edge_index = jnp.stack([src, dst])
    x = x + _L0_gnn_ref(_layernorm(x, axis=-1), edge_index, edge_type_8, L0_gnn_W_rel, L0_gnn_W_root, L0_gnn_bias)
    x = x + _L0_ffn_ref(_layernorm(x, axis=-1)[None], L0_ffn_gate_w, L0_ffn_gate_b, L0_ffn_w1, L0_ffn_b1, L0_ffn_w2, L0_ffn_b2)[0]
    return x

_drawn_inputs = setup_inputs


def setup_inputs(seed=0):
    import zlib

    import numpy as np

    out = dict(_drawn_inputs(seed))
    spreads = {'L0_ffn_gate_b': (0.0, 0.8), 'L0_ffn_b1': (0.0, 0.8), 'L0_ffn_b2': (0.0, 0.8)}
    factors = {'L0_gnn_bias': 8.0, 'L0_ffn_gate_w': 8.0, 'L0_ffn_w1': 8.0, 'L0_ffn_w2': 8.0}
    for name, (base, spread) in spreads.items():
        noise = np.random.default_rng([zlib.crc32(name.encode()), seed]).standard_normal(out[name].shape)
        drawn = base * np.exp(spread * noise) if base else spread * noise
        out[name] = jnp.asarray(drawn.astype(out[name].dtype))
    for name, factor in factors.items():
        out[name] = (out[name] * factor).astype(out[name].dtype)
    return out
```

```python
from contextlib import ExitStack

import numpy as np

import concourse.bass as bass
from concourse import mybir

F32 = mybir.dt.float32
I32 = mybir.dt.int32
ALU = mybir.AluOpType
ACT = mybir.ActivationFunctionType
AX = mybir.AxisListType

P = 128
N = 6250
D = 256
E = 100000
R = 8
L = 3
X = 8
F = 1024
CAP = -(-5 * N // (4 * X))
EPS = 1e-5
NB = -(-N // P)
NLAST = N - (NB - 1) * P
KD = D // P
RD = R * D
TILES = -(-E // P)
TC = -(-TILES // P)
U = 16
PAIRS = -(-(TILES + NB - 1) // U) * U
BODIES = PAIRS // U
HALF = PAIRS // 2
OH = 4
NOWHERE = 9999
CH = RD // 512
KF = F // P
CC = -(-CAP // P)
CLAST = CAP - (CC - 1) * P
T0 = (CAP + 1) // 2
TPARTS = ((0, T0), (T0, CAP - T0))
FLT_MAX = float(np.finfo(np.float32).max)


def ffn_gnn(nc, x, src, dst, etype, w_rel, w_root, bias, gate_w, gate_b, w1, b1, w2, b2, out):
    ctx = ExitStack()
    with ctx:
        def sb(name, shape, dt=F32):
            return ctx.enter_context(nc.sbuf_tensor(name, shape, dt))

        def sem(name):
            return ctx.enter_context(nc.semaphore(name))

        def dram(name, shape, dt=F32):
            return nc.dram_tensor(name, shape, dt, kind="Internal").ap()

        xr = dram("xr", [NB * P, RD])
        xr_rows = xr.rearrange("n (r d) -> (n r) d", r=R)
        rec = dram("rec", [E, 2], I32)
        buf = dram("buf", [X * CAP, D])
        ybuf = dram("ybuf", [X * CAP, D])

        agg = sb("agg", [P, (NB + 1) * D])
        bias_bc = sb("bias_bc", [P, L, D])
        hn = sb("hn", [P, 2, D])
        xT = sb("xT", [P, 2, KD, P])
        wroot = sb("wroot", [P, KD, D])
        onehot = sb("onehot", [P, OH, P])
        xin = sb("xin", [P, 2, D])
        tmp = sb("tmp", [P, 2, D])
        keyq = sb("keyq", [P, PAIRS + U], I32)
        dloc = sb("dloc", [P, PAIRS + OH])
        bqi = sb("bqi", [1, PAIRS], I32)
        idx = sb("idx", [P, U], I32)
        ident = sb("ident", [P, P])
        ones = sb("ones", [P, P])
        tri = sb("tri", [P, P])
        stri = sb("stri", [P, P])
        iota_n = sb("iota_n", [P, P])
        pcol = sb("pcol", [P, TC])
        bnd = sb("bnd", [P, NB + 1])
        iota_x8 = sb("iota_x8", [P, NB, X])
        xbase = sb("xbase", [P, NB, X])
        cnt = sb("cnt", [P, NB + 1])
        viol = sb("viol", [P, 1])
        flag = sb("flag", [P, 1], I32)
        edges3 = sb("edges3", [NB, 3])
        edges3i = sb("edges3i", [NB, 3], I32)
        npair = sb("npair", [NB, 1])
        delta = sb("delta", [NB, 1])
        pnext = sb("pnext", [NB, 1])
        stats = sb("stats", [P, NB, 6])
        mv = sb("mv", [P, NB, 2])
        rstd = sb("rstd", [P, NB])
        nbias = sb("nbias", [P, NB])
        eps = sb("eps", [P, 1])
        gw = sb("gw", [P, KD, X])
        gb = sb("gb", [P, X])
        mx = sb("mx", [P, NB])
        mn = sb("mn", [P, NB])
        pos = sb("pos", [P, NB])
        ebase = sb("ebase", [P, NB])
        kept = sb("kept", [P, NB])
        slot = sb("slot", [P, NB])
        pen = sb("pen", [P, NB])
        prk = sb("prk", [P, NB])
        slot_s = sb("slot_s", [P, NB], I32)
        slot_g = sb("slot_g", [P, NB], I32)
        gcol = sb("gcol", [P, 4])
        gi1 = sb("gi1", [P, 1], I32)
        gr1 = sb("gr1", [P, 2], I32)
        w1s = sb("w1s", [P, 2, KD, F])
        b1r = sb("b1r", [X * KF, P])
        b1T = sb("b1T", [P, X * KF])
        b2bc = sb("b2bc", [P, X, D])
        yfin = sb("yfin", [P, 1])
        chk = sb("chk", [P, X * CC])

        def part(t, at, shape, names=None):
            n = int(np.prod(shape))
            assert at + n <= t.shape[1]
            v = t[:, at:at + n]
            if len(shape) == 2:
                v = v.rearrange("p (a b) -> p a b", b=shape[1])
            if len(shape) == 3:
                v = v.rearrange("p (a b c) -> p a b c", b=shape[1], c=shape[2])
            return v, at + n

        mats = sb("mats", [P, KD * RD])
        wrel, _ = part(mats, 0, (KD, R, D))
        xe, _ = part(mats, 0, (2, CC, D))
        lg, at = part(mats, 0, (NB, X))
        ex, at = part(mats, at, (NB, X))
        ohx, at = part(mats, at, (NB, X))
        r1, at = part(mats, at, (NB, X))
        r2, at = part(mats, at, (NB, X))
        base, at = part(mats, at, (X, NB))
        tots, at = part(mats, at, (X, NB))
        going = sb("going", [P, 2 * RD])
        xrs, _ = part(going, 0, (2, RD))
        ye, _ = part(going, 0, (2, CC, D))
        came = sb("came", [P, U * D])
        rows, _ = part(came, 0, (U, D))
        xeT, _ = part(came, 0, (2, KD, CC * P))
        xn = sb("xn", [P, NB * D])
        hT, at = part(xn, 0, (KF, CAP))
        w2s, _ = part(xn, at, (2, KF, D))
        nd, at = part(xn, 0, (TC, P))
        nd2, at = part(xn, at, (TC, P))
        keyf, at = part(xn, at, (TC, P))
        dstf, at = part(xn, at, (TC, P))
        ns, at_nt = part(xn, at, (TC, P))
        nt, at2 = part(xn, at_nt, (TC, P))
        grec, _ = part(xn, at, (TC * P, 2))
        etmp, at = part(xn, at2, (TC * P,))
        sel, at = part(xn, at, (2, PAIRS))
        tau, at = part(xn, at, (PAIRS,))
        iota_q, at = part(xn, at, (PAIRS,))
        gscan, at_pos = part(xn, at, (TC * P,))
        bq, _ = part(xn, at, (PAIRS,))
        gpos, at = part(xn, at_pos, (TC * P,))
        gidx, at = part(xn, at, (TC * P,))
        ldelta, at = part(xn, at, (P,))
        ldelta = ldelta[0:NB, :]
        reach = sel[0:NB, 1, :]
        gmask = etmp
        nd, nd2, ns, nt, grec, gidx = (t.bitcast(I32) for t in (nd, nd2, ns, nt, grec, gidx))

        PS = ctx.enter_context(nc.psum_tensor("PS", [P, 8, 512], F32))
        SEG, TAB, CHB, ROOT, TP = 0, 2, 4, 6, 7

        x_in = [sem(f"x_in{c}") for c in range(7)]
        edges_in = sem("edges_in")
        shift_in = sem("shift_in")
        w_in = sem("w_in")
        small_in = sem("small_in")
        consts = sem("consts")
        padded = sem("padded")
        zeroed = sem("zeroed")
        stats_done = sem("stats_done")
        std_done = sem("std_done")
        norm_ready = sem("norm_ready")
        hn_ready = sem("hn_ready")
        transposed = sem("transposed")
        xT_ready = sem("xT_ready")
        chunk_ready = sem("chunk_ready")
        evac_done = sem("evac_done")
        root_ready = sem("root_ready")
        root_done = sem("root_done")
        xr_stored = [sem(f"xr_stored{h}") for h in range(2)]
        w_used = sem("w_used")
        tab_dve = sem("tab_dve")
        tab_pe = sem("tab_pe")
        gen_dve = sem("gen_dve")
        gen_pe = sem("gen_pe")
        gen_cp = sem("gen_cp")
        gen_sc = sem("gen_sc")
        gen_done = sem("gen_done")
        gen_in = sem("gen_in")
        tables = sem("tables")
        idx_ready = sem("idx_ready")
        gathered = [sem(f"gathered{u}") for u in range(U)]
        onehot_ready = sem("onehot_ready")
        pair_done = sem("pair_done")
        acc_done = sem("acc_done")
        xin_in = [sem(f"xin_in{h}") for h in range(2)]
        y_ready = sem("y_ready")
        lg_ready = sem("lg_ready")
        lg_done = sem("lg_done")
        xn_done = sem("xn_done")
        logits_done = sem("logits_done")
        exp_done = sem("exp_done")
        rt_dve = sem("rt_dve")
        rt_pe = sem("rt_pe")
        scattered = sem("scattered")
        b1_tp = sem("b1_tp")
        b1_ready = sem("b1_ready")
        xe_in = [sem(f"xe_in{h}") for h in range(2)]
        w1_in = [sem(f"w1_in{h}") for h in range(2)]
        w2_in = [sem(f"w2_in{h}") for h in range(2)]
        xe_tp = sem("xe_tp")
        xeT_ready = sem("xeT_ready")
        h_psum = sem("h_psum")
        h_ready = sem("h_ready")
        y_psum = sem("y_psum")
        ye_ready = sem("ye_ready")
        y_stored = [sem(f"y_stored{h}") for h in range(2)]
        ygot = sem("ygot")
        fin_dve = sem("fin_dve")
        fin_pe = sem("fin_pe")
        out_ready = sem("out_ready")
        stored = sem("stored")

        block = ctx.enter_context(nc.Block())

        def blk(b):
            return bass.ds(b * D, D)

        def edge_parts(a):
            n = a.shape[0]
            full = (n // (P * P)) * P * P
            whole = (n - full) // P
            return full, whole, n - full - whole * P

        def load_edges(sp, a, t, s):
            full, whole, rest = edge_parts(a)
            g = full // (P * P)
            sp.dma_start(t[:, 0:g, :], a[0:full].rearrange("(g t e) -> t g e", g=g, e=P)).then_inc(s, 16)
            sp.dma_start(t[0:whole, g, :], a[full:full + whole * P].rearrange("(t e) -> t e", e=P)).then_inc(s, 16)
            sp.dma_start(t[whole:whole + 1, g, 0:rest], a[full + whole * P:].rearrange("(t e) -> t e", t=1)).then_inc(s, 16)

        def load_mats(sp, l):
            for k in range(KD):
                sp.dma_start(wrel[:, k, :, :], w_rel[l][:, k * P:(k + 1) * P, :].rearrange("r p e -> p r e")).then_inc(w_in, 16)
            sp.dma_start(wroot[:, :, :], w_root[l].rearrange("(k p) e -> p k e", p=P)).then_inc(w_in, 16)

        @block.sync
        def _(sp):
            sp.wait_ge(padded, 1)
            for c in range(7):
                if c == 6:
                    sp.dma_start(agg[:, 42 * D:48 * D].rearrange("p (b d) -> p b d", d=D),
                                 x[42 * P:48 * P, :].rearrange("(b p) d -> p b d", p=P)).then_inc(x_in[c], 16)
                    sp.dma_start(agg[0:NLAST, 48 * D:49 * D], x[48 * P:N, :]).then_inc(x_in[c], 16)
                else:
                    sp.dma_start(agg[:, 7 * c * D:7 * (c + 1) * D].rearrange("p (b d) -> p b d", d=D),
                                 x[7 * c * P:7 * (c + 1) * P, :].rearrange("(b p) d -> p b d", p=P)).then_inc(x_in[c], 16)
                if c == 0:
                    load_mats(sp, 0)
            load_edges(sp, dst, nd, edges_in)
            load_edges(sp, src, ns, edges_in)
            load_edges(sp, etype, nt, edges_in)
            load_edges(sp, dst[1:E], nd2, edges_in)
            sp.dma_start(bias_bc[:, :, :], bias.rearrange("(o l) d -> o l d", o=1).broadcast_to([P, L, D])).then_inc(small_in, 16)
            sp.dma_start(gb[:, :], gate_b.rearrange("(o x) -> o x", o=1).broadcast_to([P, X])).then_inc(small_in, 16)
            sp.dma_start(b2bc[:, :, :], b2.rearrange("(o x) d -> o x d", o=1).broadcast_to([P, X, D])).then_inc(small_in, 16)
            sp.dma_start(gw[:, :, :], gate_w.rearrange("(k p) x -> p k x", p=P)).then_inc(small_in, 16)
            sp.dma_start(b1r[:, :], b1.rearrange("x (k f) -> (x k) f", f=P)).then_inc(small_in, 16)
            sp.wait_ge(zeroed, 1)
            sp.dma_start(buf.rearrange("s d -> (s d)").rearrange("(p r c) -> p r c", p=P, r=16),
                         came[:, 0:CAP].rearrange("p (o c) -> p o c", o=1).broadcast_to([P, 16, CAP])).then_inc(zeroed, 16)
            for e in range(2):
                sp.dma_start(w1s[:, e, :, :], w1[e].rearrange("(k p) f -> p k f", p=P)).then_inc(w1_in[e], 16)

            def store_rows(l, b, h):
                g = NB * l + b
                sp.wait_ge(evac_done, CH * g + CH)
                sp.dma_start(xr[bass.ds(b * P, P), :], xrs[:, h, :]).then_inc(xr_stored[h], 16)

            for l in range(L):
                with sp.Fori(0, NB - 2, 2) as b:
                    store_rows(l, b, l % 2)
                    store_rows(l, b + 1, (l + 1) % 2)
                store_rows(l, NB - 1, l % 2)
                if l == 0:
                    sp.wait_ge(tab_dve, 2)
                    unsorted = sp.value_load(flag[0:1, 0:1], min_val=0, max_val=E)
                    with sp.If(unsorted > 0):
                        sp.wait_ge(gen_done, 1)
                        full, whole, rest = edge_parts(dst)
                        g = full // (P * P)
                        sp.dma_start(grec[:, 0:g * P, :].rearrange("t (g e) c -> t g (e c)", g=g),
                                     rec[0:full, :].rearrange("(g t e) c -> t g (e c)", g=g, e=P)).then_inc(gen_in, 16)
                        sp.dma_start(grec[0:whole, g * P:(g + 1) * P, :].rearrange("t e c -> t (e c)"),
                                     rec[full:full + whole * P, :].rearrange("(t e) c -> t (e c)", e=P)).then_inc(gen_in, 16)
                        sp.dma_start(grec[whole:whole + 1, g * P:g * P + rest, :].rearrange("t e c -> t (e c)"),
                                     rec[full + whole * P:, :].rearrange("(t e) c -> t (e c)", t=1)).then_inc(gen_in, 16)
                if l + 1 < L:
                    sp.wait_ge(root_ready, NB * (l + 1))
                    load_mats(sp, l + 1)

            def load_x(b, h):
                n = NLAST if isinstance(b, int) and b == NB - 1 else P
                sp.dma_start(xin[0:n, h, :], x[bass.ds(b * P, n), :]).then_inc(xin_in[h], 16)

            load_x(0, 0)
            load_x(1, 1)
            with sp.Fori(2, NB - 2, 2) as b:
                sp.wait_ge(y_ready, b - 1)
                load_x(b, 0)
                sp.wait_ge(y_ready, b)
                load_x(b + 1, 1)
            sp.wait_ge(y_ready, NB - 2)
            load_x(NB - 1, 0)

            bufx = buf.rearrange("(x c) d -> x c d", x=X)
            ybx = ybuf.rearrange("(x c) d -> x c d", x=X)

            def load_tokens(e, h):
                sp.dma_start(xe[:, h, 0:CC - 1, :],
                             bufx[bass.ds(e, 1), 0:(CC - 1) * P, :].rearrange("a (c p) d -> p (a c) d", p=P)).then_inc(xe_in[h], 16)
                sp.dma_start(xe[0:CLAST, h, CC - 1, :],
                             bufx[bass.ds(e, 1), (CC - 1) * P:CAP, :].rearrange("a c d -> (a c) d")).then_inc(xe_in[h], 16)

            def load_weights(e, h):
                sp.dma_start(w1s[:, h, :, :], w1[bass.ds(e, 1), :, :].rearrange("a (k p) f -> p (a k) f", p=P)).then_inc(w1_in[h], 16)
                sp.dma_start(w2s[:, h, :, :], w2[bass.ds(e, 1), :, :].rearrange("a (k p) d -> p (a k) d", p=P)).then_inc(w2_in[h], 16)

            def store_y(e, h):
                sp.wait_ge(ye_ready, CC * e + CC)
                sp.dma_start(ybx[bass.ds(e, 1), 0:(CC - 1) * P, :].rearrange("a (c p) d -> p (a c) d", p=P),
                             ye[:, h, 0:CC - 1, :]).then_inc(y_stored[h], 16)
                sp.dma_start(ybx[bass.ds(e, 1), (CC - 1) * P:CAP, :].rearrange("a c d -> (a c) d"),
                             ye[0:CLAST, h, CC - 1, :]).then_inc(y_stored[h], 16)

            sp.wait_ge(scattered, 16 * NB)
            for e in range(2):
                sp.dma_start(w2s[:, e, :, :], w2[e].rearrange("(k p) d -> p k d", p=P)).then_inc(w2_in[e], 16)
            load_tokens(0, 0)
            load_tokens(1, 1)

            def next_expert(e, h):
                store_y(e, h)
                load_tokens(e + 2, h)
                load_weights(e + 2, h)

            with sp.Fori(0, X - 3, 2) as e:
                next_expert(e, 0)
                next_expert(e + 1, 1)
            store_y(X - 2, 0)
            store_y(X - 1, 1)

            with sp.Fori(0, NB - 1) as b:
                sp.wait_ge(out_ready, b + 1)
                sp.dma_start(out[bass.ds(b * P, P), :], agg[:, blk(b)]).then_inc(stored, 16)
            sp.wait_ge(out_ready, NB)
            sp.dma_start(out[(NB - 1) * P:N, :], agg[0:NLAST, blk(NB - 1)]).then_inc(stored, 16)
            sp.wait_ge(stored, 16 * NB)

        @block.gpsimd
        def _(pool):
            pool.memset(nd[:, TC - 1, :], NOWHERE)
            pool.memset(nd2[:, TC - 1, :], NOWHERE)
            pool.memset(ns[:, TC - 1, :], 0)
            pool.memset(nt[:, TC - 1, :], 0)
            pool.memset(agg[:, blk(NB - 1)], 0.0)
            pool.memset(agg[:, blk(NB)], 0.0).then_inc(padded, 1)
            pool.memset(ones[:, :], 1.0)
            pool.memset(tri[:, :], 1.0)
            pool.memset(stri[:, :], 1.0)
            pool.memset(ident[:, :], 1.0)
            pool.memset(eps[:, :], EPS)
            pool.memset(pen[:, :], 0.0)
            pool.drain()
            pool.affine_select(out=ident[:, :], in_=ident[:, :], compare_op=ALU.is_equal, fill=0.0, base=0,
                               pattern=[[-1, P]], channel_multiplier=1)
            pool.affine_select(out=tri[:, :], in_=tri[:, :], compare_op=ALU.is_ge, fill=0.0, base=0,
                               pattern=[[1, P]], channel_multiplier=-1)
            pool.affine_select(out=stri[:, :], in_=stri[:, :], compare_op=ALU.is_gt, fill=0.0, base=0,
                               pattern=[[1, P]], channel_multiplier=-1)
            pool.affine_select(out=pen[:, NB - 1:NB], in_=pen[:, NB - 1:NB], compare_op=ALU.is_ge,
                               fill=float(2 * X * CAP), base=NLAST - 1, pattern=[[0, 1]], channel_multiplier=-1)
            ok = dict(allow_small_or_imprecise_dtypes=True)
            pool.iota(iota_n[:, :], pattern=[[1, P]], base=0, channel_multiplier=0, **ok)
            pool.iota(iota_q[:, :], pattern=[[1, PAIRS]], base=0, channel_multiplier=0, **ok)
            pool.iota(pcol[:, :], pattern=[[P, TC]], base=0, channel_multiplier=1, **ok)
            pool.iota(bnd[:, :], pattern=[[P, NB + 1]], base=0, channel_multiplier=0, **ok)
            pool.iota(iota_x8[:, :, :], pattern=[[0, NB], [1, X]], base=-X, channel_multiplier=0, **ok)
            pool.iota(xbase[:, :, :], pattern=[[0, NB], [CAP, X]], base=0, channel_multiplier=0, **ok)
            pool.drain()
            pool.sem_inc(consts, 1)
            pool.memset(came[:, 0:CAP], 0.0).then_inc(zeroed, 1)

            pool.wait_ge(tab_dve, 2)
            unsorted = pool.value_load(flag[0:1, 0:1], min_val=0, max_val=E)
            with pool.If(unsorted > 0):
                with pool.Fori(0, TC * P) as c:
                    pool.wait_ge(gen_cp, c + 1)
                    pool.nop(nofuse=True)
                    pool.indirect_dma_start(out=rec, out_offset=bass.IndirectOffsetOnAxis(ap=gi1[:, :], axis=0),
                                            in_=gr1[:, :], in_offset=None,
                                            bounds_check=E - 1, oob_is_err=False).then_inc(gen_sc, 16)
                    pool.wait_ge(gen_sc, 16 * c + 16)
                pool.sem_inc(gen_done, 1)

            for l in range(L):
                pool.wait_ge(tables, 1)
                pool.wait_ge(zeroed, 17)
                for h in range(2):
                    pool.wait_ge(xr_stored[h], 16 * ((NB * (l + 1) + 1 - h) // 2))
                with pool.Fori(0, BODIES) as i:
                    for u in range(U):
                        if u % (U // 2) == 0:
                            pool.wait_ge(idx_ready, 2 * BODIES * l + 2 * i + 1 + u // (U // 2))
                            pool.nop(nofuse=True)
                        pool.wait_ge(pair_done, PAIRS * l + U * i + u + 1)
                        pool.nop(nofuse=True)
                        pool.indirect_dma_start(out=rows[:, u, :], out_offset=None, in_=xr_rows,
                                                in_offset=bass.IndirectOffsetOnAxis(ap=idx[:, u:u + 1], axis=0)
                                                ).then_inc(gathered[u], 16)

            pool.wait_ge(rt_dve, 3)
            pool.wait_ge(zeroed, 17)
            for b in range(NB):
                pool.indirect_dma_start(out=buf, out_offset=bass.IndirectOffsetOnAxis(ap=slot_s[:, b:b + 1], axis=0),
                                        in_=xn[:, b * D:(b + 1) * D], in_offset=None,
                                        bounds_check=X * CAP - 1, oob_is_err=False).then_inc(scattered, 16)
            for h in range(2):
                pool.wait_ge(y_stored[h], 32 * X // 2)
            for b in range(NB):
                pool.indirect_dma_start(out=xn[:, b * D:(b + 1) * D], out_offset=None, in_=ybuf,
                                        in_offset=bass.IndirectOffsetOnAxis(ap=slot_g[:, b:b + 1], axis=0)
                                        ).then_inc(ygot, 16)

        @block.scalar
        def _(act):
            def std(lo, hi):
                act.activation(rstd[:, lo:hi], mv[:, lo:hi, 1], ACT.Sqrt, bias=eps[:, :]).then_inc(std_done, 1)

            def norm(b, h, g):
                if not (isinstance(g, int) and g < 2):
                    act.wait_ge(transposed, g - 1)
                    act.nop(nofuse=True)
                act.activation(hn[:, h, :], agg[:, blk(b)], ACT.Identity,
                               bias=nbias[:, bass.ds(b, 1)], scale=rstd[:, bass.ds(b, 1)]).then_inc(hn_ready, 1)

            def copy_T(g, h, func):
                act.wait_ge(transposed, g + 1)
                if not (isinstance(g, int) and g < 2):
                    act.wait_ge(root_ready, g - 1)
                act.activation(xT[:, h, :, :].rearrange("p k n -> p (k n)"), PS[:, TP, 0:D], func).then_inc(xT_ready, 1)

            def evac(b, g, h):
                if not (isinstance(g, int) and g < 2):
                    act.wait_ge(xr_stored[h], 16 * (g // 2) if isinstance(g, int) else 8 * (g - h))
                for k in range(CH):
                    act.wait_ge(chunk_ready, CH * g + k + 1)
                    act.copy(xrs[:, h, 512 * k:512 * (k + 1)], PS[:, CHB + k % 2, :]).then_inc(evac_done, 1)
                act.wait_ge(root_ready, g + 1)
                act.copy(agg[:, blk(b)], PS[:, ROOT, 0:D]).then_inc(root_done, 1)

            act.wait_ge(consts, 1)
            act.wait_ge(stats_done, 1)
            std(0, 7)
            act.wait_ge(norm_ready, 1)
            for l in range(L):
                func = ACT.Copy if l == 0 else ACT.Relu
                ahead = l == 0

                def body(b, par, n2=True, n1=True):
                    g = NB * l + b
                    if ahead and n2:
                        norm(b + 2, par, g + 2)
                    if n1:
                        copy_T(g + 1, 1 - par, func)
                    evac(b, g, par)

                if ahead:
                    norm(0, 0, 0)
                    norm(1, 1, 1)
                copy_T(NB * l, l % 2, func)
                for b in range(4):
                    body(b, (b + l) % 2)
                if ahead:
                    act.wait_ge(stats_done, 2)
                    std(7, NB)
                    act.wait_ge(norm_ready, 2)
                with act.Fori(4, NB - 4, 2) as b:
                    body(b, l % 2)
                    body(b + 1, (l + 1) % 2)
                body(NB - 3, l % 2)
                body(NB - 2, (l + 1) % 2, n2=False)
                body(NB - 1, l % 2, n2=False, n1=False)

                if l == 0:
                    act.wait_ge(tables, 1)
                    act.copy(idx[:, :], keyq[:, 0:U])
                    act.drain()
                    act.sem_inc(idx_ready, 2)
                with act.Fori(0, BODIES) as i:
                    for hh in range(2):
                        for u in range(hh * U // 2, (hh + 1) * U // 2):
                            act.wait_ge(gathered[u], 16 * (BODIES * l + i + 1))
                        act.copy(idx[:, hh * U // 2:(hh + 1) * U // 2],
                                 keyq[:, bass.ds(U * i + U + hh * U // 2, U // 2)]).then_inc(idx_ready, 1)

            act.wait_ge(y_ready, NB)
            act.wait_ge(stats_done, 3)
            std(0, NB)
            act.wait_ge(norm_ready, 3)
            g0 = NB * L

            def logits(b, par, n2=True, n1=True):
                g = g0 + b
                if n2:
                    norm(b + 2, par, g + 2)
                if n1:
                    copy_T(g + 1, 1 - par, ACT.Copy)

            norm(0, g0 % 2, g0)
            norm(1, 1 - g0 % 2, g0 + 1)
            copy_T(g0, g0 % 2, ACT.Copy)
            with act.Fori(0, NB - 4, 2) as b:
                logits(b, g0 % 2)
                logits(b + 1, 1 - g0 % 2)
            logits(NB - 3, g0 % 2)
            logits(NB - 2, 1 - g0 % 2, n2=False)
            act.wait_ge(rt_dve, 1)
            act.activation(ex[:, :, :], r1[:, :, :], ACT.Exp).then_inc(exp_done, 1)

            def hidden(e, h):
                for k in range(KF):
                    for t, (t0, tn) in enumerate(TPARTS):
                        j = 2 * k + t
                        act.wait_ge(h_psum, 2 * KF * e + j + 1)
                        act.nop(nofuse=True)
                        act.activation(hT[:, k, t0:t0 + tn], PS[:, SEG + j % 4, 0:tn], ACT.Relu,
                                       bias=b1T[:, bass.ds(KF * e + k, 1)]).then_inc(h_ready, 1)

            act.wait_ge(b1_ready, 1)
            with act.Fori(0, X) as e:
                hidden(e, 0)

        @block.vector
        def _(dve):
            def block_stats(b):
                dve.bn_stats(stats[:, bass.ds(b, 1), :].rearrange("p a s -> p (a s)"), agg[:, blk(b)])

            def aggregate(lo, hi, n):
                dve.drain()
                for b in range(lo, hi):
                    dve.bn_aggr(mv[:, b, :], stats[:, b, :])
                dve.drain()
                dve.sem_inc(stats_done, 1)

            def finish_norm(lo, hi, n):
                dve.wait_ge(std_done, n)
                dve.reciprocal(rstd[:, lo:hi], rstd[:, lo:hi])
                dve.drain()
                dve.scalar_tensor_tensor(nbias[:, lo:hi], mv[:, lo:hi, 0], -1.0, rstd[:, lo:hi],
                                         op0=ALU.mult, op1=ALU.mult).then_inc(norm_ready, 1)

            dve.wait_ge(x_in[0], 16)
            with dve.Fori(0, 7) as b:
                block_stats(b)
            aggregate(0, 7, 1)
            finish_norm(0, 7, 1)
            for c in range(1, 7):
                dve.wait_ge(x_in[c], 32 if c == 6 else 16)
                with dve.Fori(7 * c, 7 * c + 7) as b:
                    block_stats(b)
            aggregate(7, NB, 2)
            finish_norm(7, NB, 2)

            dve.wait_ge(consts, 1)
            dve.wait_ge(edges_in, 16 * 12)
            flat = lambda t: t[:, :, :].rearrange("p g e -> p (g e)")
            dve.scalar_tensor_tensor(flat(keyf), flat(ns), float(R), flat(nt), op0=ALU.mult, op1=ALU.add)
            dve.tensor_copy(flat(dstf), flat(nd))
            dve.tensor_tensor(etmp[:, :], flat(nd), flat(nd2), ALU.is_gt)
            dve.drain()
            dve.reduce_sum(viol[:, :], etmp[:, :], axis=AX.X)
            dve.memset(cnt[:, 0:1], 0.0)
            dve.drain()
            with dve.Fori(1, NB + 1) as j:
                dve.tensor_scalar(etmp[:, :], flat(dstf), bnd[:, bass.ds(j, 1)], None, op0=ALU.is_lt, op1=ALU.add,
                                  accum_out=cnt[:, bass.ds(j, 1)])
                dve.drain()
            dve.sem_inc(tab_dve, 1)
            dve.wait_ge(tab_pe, 1)
            dve.tensor_copy(flag[:, :], PS[:, TAB, 256:257])
            dve.drain()
            dve.sem_inc(tab_dve, 1)
            unsorted = dve.value_load(flag[0:1, 0:1], min_val=0, max_val=E)
            with dve.If(unsorted > 0):
                dve.memset(gpos[:, :], 0.0)
                dve.memset(gcol[:, :], 0.0)
                dve.tensor_scalar(gidx[:, :], flat(nd), 7, None, op0=ALU.arith_shift_right)
                dve.drain()
                dve.tensor_copy(gscan[:, :], gidx[:, :])
                dve.drain()
                dve.tensor_copy(flat(nd2).bitcast(F32), gscan[:, :])
                dve.drain()
                with dve.Fori(0, NB) as b:
                    dve.tensor_scalar(gmask[:, :], flat(nd2).bitcast(F32), gcol[:, 0:1], None, op0=ALU.is_equal)
                    dve.drain()
                    dve.tensor_tensor_scan(gscan[:, :], gmask[:, :], gmask[:, :], 0.0, op0=ALU.add, op1=ALU.bypass)
                    dve.drain()
                    dve.sem_inc(gen_dve, 1)
                    dve.wait_ge(gen_pe, b + 1)
                    dve.scalar_tensor_tensor(gcol[:, 1:2], PS[:, TAB, 260:261], -1.0, gcol[:, 2:3],
                                             op0=ALU.add, op1=ALU.add)
                    dve.drain()
                    dve.scalar_tensor_tensor(gscan[:, :], gscan[:, :], gcol[:, 1:2], gmask[:, :],
                                             op0=ALU.add, op1=ALU.mult)
                    dve.tensor_tensor(gcol[:, 2:3], gcol[:, 2:3], PS[:, TAB, 264:265], ALU.add)
                    dve.tensor_scalar(gcol[:, 0:1], gcol[:, 0:1], 1.0, None, op0=ALU.add)
                    dve.drain()
                    dve.tensor_tensor(gpos[:, :], gpos[:, :], gscan[:, :], ALU.add)
                    dve.drain()
                dve.tensor_scalar(gmask[:, :], flat(dstf), float(NB * P), float(4 * E), op0=ALU.is_ge, op1=ALU.mult)
                dve.drain()
                dve.tensor_tensor(gpos[:, :], gpos[:, :], gmask[:, :], ALU.add)
                dve.tensor_copy(grec[:, :, 0], flat(keyf))
                dve.tensor_copy(grec[:, :, 1], flat(dstf))
                dve.drain()
                dve.tensor_copy(gidx[:, :], gpos[:, :])
                dve.drain()
                dve.tensor_copy(gi1[:, :], gidx[:, 0:1])
                dve.tensor_copy(gr1[:, :], grec[:, 0, :])
                dve.drain()
                dve.sem_inc(gen_cp, 1)
                with dve.Fori(1, TC * P) as c:
                    dve.wait_ge(gen_sc, 16 * c)
                    dve.tensor_copy(gi1[:, :], gidx[:, bass.ds(c, 1)])
                    dve.tensor_copy(gr1[:, :], grec[:, bass.ds(c, 1), :].rearrange("p a c -> p (a c)"))
                    dve.drain()
                    dve.sem_inc(gen_cp, 1)
                dve.wait_ge(gen_sc, 16 * TC * P)
                dve.wait_ge(gen_in, 48)
                dve.tensor_copy(flat(keyf), grec[:, :, 0])
                dve.tensor_copy(flat(dstf), grec[:, :, 1])
                dve.drain()

            dve.tensor_copy(edges3[:, 0:1], PS[0:NB, TAB, 257:258])
            dve.tensor_copy(edges3[:, 2:3], PS[0:NB, TAB, 258:259])
            dve.drain()
            dve.scalar_tensor_tensor(edges3[:, 1:2], edges3[:, 2:3], -1.0, edges3[:, 0:1], op0=ALU.add, op1=ALU.max)
            dve.drain()
            dve.tensor_copy(edges3i[:, :], edges3[:, :])
            dve.drain()
            dve.tensor_scalar(edges3i[:, :], edges3i[:, :], 7, None, op0=ALU.arith_shift_right)
            dve.drain()
            dve.tensor_copy(edges3[:, :], edges3i[:, :])
            dve.drain()
            dve.scalar_tensor_tensor(npair[:, :], edges3[:, 1:2], 1.0, edges3[:, 0:1], op0=ALU.add, op1=ALU.subtract)
            dve.scalar_tensor_tensor(delta[:, :], edges3[:, 2:3], -1.0, edges3[:, 1:2], op0=ALU.add, op1=ALU.subtract)
            dve.drain()
            dve.tensor_scalar(ldelta[:, :], ones[0:NB, :], delta[:, 0:1], None, op0=ALU.mult)
            dve.drain()
            dve.sem_inc(tab_dve, 1)
            dve.wait_ge(tab_pe, 2)
            dve.tensor_copy(pnext[:, :], PS[0:NB, TAB, 259:260])
            dve.drain()
            dve.tensor_scalar(reach[:, :], iota_q[0:NB, :], pnext[:, 0:1], None, op0=ALU.is_ge).then_inc(tab_dve, 1)
            dve.wait_ge(tab_pe, 3)
            for j in range(2):
                s = slice(j * HALF, (j + 1) * HALF)
                dve.tensor_copy(bq[:, s], PS[:, SEG + j, 0:HALF])
                dve.tensor_copy(bqi[:, s], PS[0:1, SEG + j, 0:HALF])
                dve.tensor_tensor(tau[:, s], PS[:, SEG + 2 + j, 0:HALF], iota_q[:, s], ALU.add)
            dve.drain()
            for c in range(TC):
                if c >= 2:
                    dve.wait_ge(tab_pe, 2 + c)
                dve.tensor_scalar(sel[:, c % 2, :], tau[:, :], pcol[:, c:c + 1], None,
                                  op0=ALU.is_equal).then_inc(tab_dve, 1)
            dve.wait_ge(tab_pe, 3 + TC)
            for j in range(2):
                s = slice(j * HALF, (j + 1) * HALF)
                dve.tensor_copy(keyq[:, s], PS[:, SEG + j, 0:HALF])
                dve.scalar_tensor_tensor(dloc[:, s], bq[:, s], float(-P), PS[:, SEG + 2 + j, 0:HALF],
                                         op0=ALU.mult, op1=ALU.add)
            dve.drain()
            dve.tensor_copy(keyq[:, PAIRS:], keyq[:, 0:U])
            dve.tensor_copy(dloc[:, PAIRS:], dloc[:, 0:OH])
            dve.drain()
            dve.sem_inc(tables, 1)

            def edge_matrix(col, s):
                dve.tensor_scalar(onehot[:, s, :], iota_n[:, :], dloc[:, col], None,
                                  op0=ALU.is_equal).then_inc(onehot_ready, 1)

            for s in range(OH):
                edge_matrix(slice(s, s + 1), s)
            dve.sem_inc(acc_done, 1)
            for l in range(L):
                if l > 0:
                    def pre(b, g, h):
                        dve.wait_ge(transposed, g - 1)
                        dve.tensor_tensor(hn[:, h, :], agg[:, blk(b)], bias_bc[:, l - 1, :],
                                          ALU.add).then_inc(hn_ready, 1)
                    dve.drain()
                    with dve.Fori(0, NB - 2, 2) as b:
                        pre(b, NB * l + b, l % 2)
                        pre(b + 1, NB * l + b + 1, (l + 1) % 2)
                    pre(NB - 1, NB * (l + 1) - 1, l % 2)
                else:
                    dve.wait_ge(small_in, 16 * 5)
                dve.wait_ge(root_done, NB * (l + 1))
                with dve.Fori(0, BODIES) as i:
                    _, blocks = nc.values_load_multi_w_load_instructions(
                        bqi[0:1, bass.ds(U * i, U)], engines=[mybir.EngineType.DVE], min_val=0, max_val=NB,
                        skip_runtime_bounds_check_because="a pair's block is a count of at most NB comparisons")
                    for u in range(U):
                        q = PAIRS * l + U * i + u
                        dve.wait_ge(pair_done, q + U + 1)
                        dve.wait_ge(acc_done, q + 1)
                        dve.tensor_tensor(agg[:, blk(blocks[u])], agg[:, blk(blocks[u])],
                                          PS[:, SEG + u % OH, 0:D], ALU.add).then_inc(acc_done, 1)
                        edge_matrix(bass.ds(U * i + u + OH, 1), u % OH)

            dve.drain()

            def residual(b, h, n):
                dve.tensor_tensor(tmp[:, h, :], agg[:, blk(b)], bias_bc[:, L - 1, :], ALU.add)
                dve.drain()
                dve.wait_ge(xin_in[h], n)
                dve.scalar_tensor_tensor(agg[:, blk(b)], tmp[:, h, :], 0.0, xin[:, h, :],
                                         op0=ALU.max, op1=ALU.add).then_inc(y_ready, 1)
                dve.drain()
                block_stats(b)

            with dve.Fori(0, NB - 2, 2) as b:
                residual(b, 0, 8 * b + 16)
                residual(b + 1, 1, 8 * b + 16)
            residual(NB - 1, 0, 8 * (NB - 1) + 16)
            aggregate(0, NB, 3)
            finish_norm(0, NB, 3)
            dve.drain()
            g0 = NB * L

            def take_logits(b):
                dve.tensor_scalar(xn[:, blk(b)], agg[:, blk(b)], rstd[:, bass.ds(b, 1)], nbias[:, bass.ds(b, 1)],
                                  op0=ALU.mult, op1=ALU.add)
                dve.wait_ge(root_ready, g0 + b + 1)
                dve.tensor_tensor(lg[:, bass.ds(b, 1), :].rearrange("p a x -> p (a x)"), PS[:, ROOT, 0:X], gb[:, :],
                                  ALU.add).then_inc(root_done, 1)

            with dve.Fori(0, NB) as b:
                take_logits(b)
            dve.drain()
            dve.tensor_reduce(mx[:, :], lg[:, :, :], axis=AX.X, op=ALU.max)
            dve.drain()
            mxb = mx[:, :].rearrange("p (b o) -> p b o", o=1).broadcast_to([P, NB, X])
            dve.tensor_tensor(r1[:, :, :], lg[:, :, :], mxb, ALU.subtract)
            dve.drain()
            dve.sem_inc(rt_dve, 1)
            dve.scalar_tensor_tensor(r2[:, :, :].rearrange("p b x -> p (b x)"), r1[:, :, :].rearrange("p b x -> p (b x)"),
                                     0.0, iota_x8[:, :, :].rearrange("p b x -> p (b x)"), op0=ALU.is_equal, op1=ALU.mult)
            dve.drain()
            dve.tensor_reduce(mn[:, :], r2[:, :, :], axis=AX.X, op=ALU.min)
            dve.drain()
            mnb = mn[:, :].rearrange("p (b o) -> p b o", o=1).broadcast_to([P, NB, X])
            dve.tensor_tensor(ohx[:, :, :], iota_x8[:, :, :], mnb, ALU.is_equal)
            dve.drain()
            dve.sem_inc(rt_dve, 1)
            dve.wait_ge(rt_pe, 1)
            dve.tensor_copy(tots[:, :, :], PS[:, SEG + 1, 0:NB * X].rearrange("p (b x) -> p x b", x=X))
            dve.drain()
            for e in range(X):
                dve.tensor_tensor_scan(base[:, e, :], tots[:, e, :], tots[:, e, :], 0.0, op0=ALU.add, op1=ALU.bypass)
            dve.drain()
            dve.tensor_tensor(base[:, :, :], base[:, :, :], tots[:, :, :], ALU.subtract)
            dve.drain()
            dve.wait_ge(exp_done, 1)
            dve.tensor_tensor(r1[:, :, :], base[:, :, :].rearrange("p x b -> p b x"),
                              PS[:, SEG, 0:NB * X].rearrange("p (b x) -> p b x", x=X), ALU.add)
            dve.tensor_tensor(r2[:, :, :], ohx[:, :, :], xbase[:, :, :], ALU.mult)
            dve.tensor_reduce(prk[:, :], ex[:, :, :], axis=AX.X, op=ALU.add)
            dve.drain()
            dve.tensor_tensor(r1[:, :, :], r1[:, :, :], ohx[:, :, :], ALU.mult)
            dve.tensor_reduce(ebase[:, :], r2[:, :, :], axis=AX.X, op=ALU.add)
            dve.reciprocal(prk[:, :], prk[:, :])
            dve.drain()
            dve.tensor_reduce(pos[:, :], r1[:, :, :], axis=AX.X, op=ALU.add)
            dve.drain()
            dve.tensor_scalar(kept[:, :], pos[:, :], float(CAP), None, op0=ALU.is_le)
            dve.scalar_tensor_tensor(slot[:, :], pos[:, :], -1.0, ebase[:, :], op0=ALU.add, op1=ALU.add)
            dve.tensor_scalar(mn[:, :], pos[:, :], float(CAP), float(2 * X * CAP), op0=ALU.is_gt, op1=ALU.mult)
            dve.tensor_scalar(mx[:, :], pos[:, :], float(CAP), -1.0, op0=ALU.min, op1=ALU.add)
            dve.drain()
            dve.tensor_tensor(slot[:, :], slot[:, :], mn[:, :], ALU.add)
            dve.tensor_tensor(mx[:, :], mx[:, :], ebase[:, :], ALU.add)
            dve.tensor_tensor(prk[:, :], prk[:, :], kept[:, :], ALU.mult)
            dve.drain()
            dve.tensor_tensor(slot[:, :], slot[:, :], pen[:, :], ALU.add)
            dve.tensor_copy(slot_g[:, :], mx[:, :])
            dve.drain()
            dve.tensor_copy(slot_s[:, :], slot[:, :])
            dve.drain()
            dve.sem_inc(rt_dve, 1)
            dve.wait_ge(b1_tp, 1)
            dve.tensor_copy(b1T[:, :], PS[:, CHB, 0:X * KF]).then_inc(b1_ready, 1)

            def take_tokens(e, h):
                for k in range(KD):
                    for c4 in range(CC // 4):
                        j = 2 * k + c4
                        n = 4 * P if c4 == 0 else CAP - 4 * P
                        dve.wait_ge(xe_tp, 4 * e + j + 1)
                        dve.tensor_copy(xeT[:, h, k, 4 * P * c4:4 * P * c4 + n], PS[:, ROOT + j % 2, 0:n]).then_inc(xeT_ready, 1)

            def take_y(e, h, c):
                n = P if c < CC - 1 else CLAST
                dve.wait_ge(y_psum, CC * e + c + 1)
                dve.tensor_tensor(ye[0:n, h, c, :], PS[0:n, CHB + c % 2, 0:D],
                                  b2bc[0:n, bass.ds(e, 1), :].rearrange("p a d -> p (a d)"), ALU.add).then_inc(ye_ready, 1)

            def expert(e, h, more=True, first=False):
                if more:
                    take_tokens(e + 1, 1 - h)
                if not first:
                    dve.wait_ge(y_stored[h], 32 * (e // 2) if isinstance(e, int) else 16 * (e - h))
                for c in range(CC):
                    take_y(e, h, c)
                dve.drain()
                for c in range(CC):
                    n = P if c < CC - 1 else CLAST
                    dve.tensor_scalar(tmp[0:n, c % 2, :], ye[0:n, h, c, :], 0.0, None, op0=ALU.mult, op1=ALU.add,
                                      accum_out=chk[0:n, bass.ds(CC * e + c, 1)])
                    dve.drain()

            dve.tensor_scalar(mn[:, :], prk[:, :], 0.0, None, op0=ALU.mult, op1=ALU.add, accum_out=yfin[:, :])
            dve.memset(chk[:, :], 0.0)
            dve.drain()
            take_tokens(0, 0)
            expert(0, 0, first=True)
            expert(1, 1, first=True)
            with dve.Fori(2, X - 3, 2) as e:
                expert(e, 0)
                expert(e + 1, 1)
            expert(X - 2, 0)
            expert(X - 1, 1, more=False)
            dve.tensor_reduce(viol[:, :], chk[:, :], axis=AX.X, op=ALU.add)
            dve.drain()
            dve.tensor_tensor(yfin[:, :], yfin[:, :], viol[:, :], ALU.add)
            dve.drain()
            dve.sem_inc(fin_dve, 1)
            dve.wait_ge(fin_pe, 1)
            dve.tensor_scalar(flag[:, :], PS[:, TP, 0:1], 0.0, None, op0=ALU.is_equal)
            dve.drain()
            finite = dve.value_load(flag[0:1, 0:1], min_val=0, max_val=1)

            with dve.If(finite < 1):
                with dve.Fori(0, NB) as b:
                    dve.wait_ge(ygot, 16 * NB)
                    t, m, v = xin[:, 0, :], xin[:, 1, :].bitcast(I32), tmp[:, 0, :]
                    dve.tensor_scalar(t, xn[:, blk(b)], prk[:, bass.ds(b, 1)], None, op0=ALU.mult)
                    dve.drain()
                    for value, test, ref in ((0.0, ALU.not_equal, None), (10000.0, ALU.is_gt, FLT_MAX),
                                             (-10000.0, ALU.is_lt, -FLT_MAX)):
                        dve.memset(v, value)
                        if ref is None:
                            dve.tensor_tensor(m, t, t, test)
                        else:
                            dve.tensor_scalar(m, t, ref, None, op0=test)
                        dve.drain()
                        dve.copy_predicated(t, m, v)
                        dve.drain()
                    dve.tensor_copy(xn[:, blk(b)], t)
                    dve.drain()
                dve.memset(prk[:, :], 1.0)
                dve.drain()
            with dve.Fori(0, NB) as b:
                dve.wait_ge(ygot, 16 * NB)
                dve.scalar_tensor_tensor(agg[:, blk(b)], xn[:, blk(b)], prk[:, bass.ds(b, 1)], agg[:, blk(b)],
                                         op0=ALU.mult, op1=ALU.add).then_inc(out_ready, 1)

        @block.tensor
        def _(pe):
            def transposes(g, h):
                pe.wait_ge(hn_ready, g + 1)
                if not (isinstance(g, int) and g < 1):
                    pe.wait_ge(xT_ready, g)
                for k in range(KD):
                    last = pe.transpose(PS[:, TP, k * P:(k + 1) * P], hn[:, h, k * P:(k + 1) * P], ident[:, :])
                last.then_inc(transposed, 1)

            def products(g, h):
                pe.wait_ge(xT_ready, g + 1)
                for c in range(CH):
                    if not (isinstance(g, int) and CH * g + c < 2):
                        pe.wait_ge(evac_done, CH * g + c - 1)
                    for k in range(KD):
                        last = pe.matmul(PS[:, CHB + c % 2, :], xT[:, h, k, :],
                                         wrel[:, k, 2 * c:2 * c + 2, :].rearrange("p r e -> p (r e)"),
                                         start=(k == 0), stop=(k == KD - 1))
                    last.then_inc(chunk_ready, 1)
                if not (isinstance(g, int) and g < 1):
                    pe.wait_ge(root_done, g)
                for k in range(KD):
                    last = pe.matmul(PS[:, ROOT, 0:D], xT[:, h, k, :], wroot[:, k, :],
                                     start=(k == 0), stop=(k == KD - 1))
                last.then_inc(root_ready, 1)

            pe.sem_inc(pair_done, U)
            pe.wait_ge(consts, 1)

            def table_a():
                pe.wait_ge(tab_dve, 1)
                pe.wait_ge(xT_ready, 25)
                pe.matmul(PS[:, TAB, 256:257], ones[:, :], viol[:, :], start=True, stop=True)
                pe.matmul(PS[0:NB, TAB, 257:258], cnt[:, 0:NB], ones[:, 0:1], start=True, stop=True)
                pe.matmul(PS[0:NB, TAB, 258:259], cnt[:, 1:NB + 1], ones[:, 0:1], start=True, stop=True).then_inc(tab_pe, 1)
                pe.wait_ge(tab_dve, 2)
                unsorted = pe.value_load(flag[0:1, 0:1], min_val=0, max_val=E)
                with pe.If(unsorted > 0):
                    with pe.Fori(0, NB) as b:
                        pe.wait_ge(gen_dve, b + 1)
                        pe.matmul(PS[:, TAB, 260:261], stri[:, :], gscan[:, TC * P - 1:TC * P], start=True, stop=True)
                        pe.matmul(PS[:, TAB, 264:265], ones[:, :], gscan[:, TC * P - 1:TC * P], start=True,
                                  stop=True).then_inc(gen_pe, 1)

            def table_b():
                pe.wait_ge(tab_dve, 3)
                pe.matmul(PS[0:NB, TAB, 259:260], tri[0:NB, 0:NB], npair[:, :], start=True, stop=True).then_inc(tab_pe, 1)

            def table_c():
                pe.wait_ge(tab_dve, 4)
                for j in range(2):
                    s = slice(j * HALF, (j + 1) * HALF)
                    pe.matmul(PS[:, SEG + j, 0:HALF], ones[0:NB, :], reach[:, s], start=True, stop=True)
                    last = pe.matmul(PS[:, SEG + 2 + j, 0:HALF], ldelta[:, :], reach[:, s], start=True, stop=True)
                last.then_inc(tab_pe, 1)

            def table_d():
                for c in range(TC):
                    pe.wait_ge(tab_dve, 5 + c)
                    for j in range(2):
                        s = slice(j * HALF, (j + 1) * HALF)
                        pe.matmul(PS[:, SEG + j, 0:HALF], keyf[:, c, :], sel[:, c % 2, s], start=(c == 0), stop=(c == TC - 1))
                        last = pe.matmul(PS[:, SEG + 2 + j, 0:HALF], dstf[:, c, :], sel[:, c % 2, s],
                                         start=(c == 0), stop=(c == TC - 1))
                    last.then_inc(tab_pe, 1)

            for l in range(L):
                pe.wait_ge(w_in, 16 * (KD + 1) * (l + 1))

                def body(b, par, n1=True):
                    g = NB * l + b
                    if n1:
                        transposes(g + 1, 1 - par)
                    products(g, par)

                transposes(NB * l, l % 2)
                body(0, l % 2)
                body(1, (l + 1) % 2)

                def run(lo, hi):
                    with pe.Fori(lo, hi - 1, 2) as b:
                        body(b, l % 2)
                        body(b + 1, (l + 1) % 2)

                if l == 0:
                    run(2, 24)
                    table_a()
                    run(24, 28)
                    table_b()
                    run(28, 32)
                    table_c()
                    run(32, 36)
                    table_d()
                    run(36, NB - 1)
                else:
                    run(2, NB - 1)
                body(NB - 1, l % 2, n1=False)

                if l == 0:
                    pe.wait_ge(tables, 1)
                with pe.Fori(0, BODIES) as i:
                    for u in range(U):
                        q = PAIRS * l + U * i + u
                        pe.wait_ge(onehot_ready, q + 1)
                        pe.wait_ge(gathered[u], 16 * (BODIES * l + i + 1))
                        pe.matmul(PS[:, SEG + u % OH, 0:D], onehot[:, u % OH, :], rows[:, u, :],
                                  start=True, stop=True).then_inc(pair_done, 1)

            g0 = NB * L
            pe.wait_ge(small_in, 16 * 5)

            def logit(b, par, n1=True):
                g = g0 + b
                if n1:
                    transposes(g + 1, 1 - par)
                pe.wait_ge(xT_ready, g + 1)
                pe.wait_ge(root_done, g)
                for k in range(KD):
                    last = pe.matmul(PS[:, ROOT, 0:X], xT[:, par, k, :], gw[:, k, :], start=(k == 0), stop=(k == KD - 1))
                last.then_inc(root_ready, 1)

            transposes(g0, g0 % 2)
            with pe.Fori(0, NB - 2, 2) as b:
                logit(b, g0 % 2)
                logit(b + 1, 1 - g0 % 2)
            logit(NB - 1, g0 % 2, n1=False)
            pe.wait_ge(rt_dve, 2)
            oh2 = ohx[:, :, :].rearrange("p b x -> p (b x)")
            pe.matmul(PS[:, SEG, 0:NB * X], tri[:, :], oh2, start=True, stop=True)
            pe.matmul(PS[:, SEG + 1, 0:NB * X], ones[:, :], oh2, start=True, stop=True).then_inc(rt_pe, 1)
            pe.transpose(PS[:, CHB, 0:X * KF], b1r[:, :], ident[0:X * KF, 0:X * KF]).then_inc(b1_tp, 1)

            def tokens(e, h):
                pe.wait_ge(xe_in[h], 32 * (e // 2 + 1) if isinstance(e, int) else 16 * (e - h) + 32)
                for k in range(KD):
                    for c4 in range(CC // 4):
                        j = 2 * k + c4
                        if not (isinstance(e, int) and 4 * e + j < 2):
                            pe.wait_ge(xeT_ready, 4 * e + j - 1)
                        for c in range(4 * c4, 4 * c4 + 4):
                            n = P if c < CC - 1 else CLAST
                            last = pe.transpose(PS[:, ROOT + j % 2, (c % 4) * P:(c % 4) * P + n],
                                                xe[0:n, h, c, k * P:(k + 1) * P], ident[0:n, 0:n])
                        last.then_inc(xe_tp, 1)

            def mm_expert(e, h, more=True):
                half = (e // 2 + 1) if isinstance(e, int) else None
                pe.wait_ge(w1_in[h], 16 * half if half else 8 * (e - h) + 16)
                pe.wait_ge(xeT_ready, 4 * e + 4)
                for k in range(KF):
                    for t, (t0, tn) in enumerate(TPARTS):
                        j = 2 * k + t
                        if not (isinstance(e, int) and e == 0 and j < 4):
                            pe.wait_ge(h_ready, 2 * KF * e + j - 3)
                        for kk in range(KD):
                            last = pe.matmul(PS[:, SEG + j % 4, 0:tn], w1s[:, h, kk, k * P:(k + 1) * P],
                                             xeT[:, h, kk, t0:t0 + tn], start=(kk == 0), stop=(kk == KD - 1))
                        last.then_inc(h_psum, 1)
                if more:
                    tokens(e + 1, 1 - h)
                pe.wait_ge(w2_in[h], 16 * half if half else 8 * (e - h) + 16)
                pe.wait_ge(h_ready, 2 * KF * e + 2 * KF)
                for c in range(CC):
                    n = P if c < CC - 1 else CLAST
                    if isinstance(e, int) and CC * e + c < 2:
                        pe.wait_ge(b1_ready, 1)
                    else:
                        pe.wait_ge(ye_ready, CC * e + c - 1)
                    for k in range(KF):
                        last = pe.matmul(PS[0:n, CHB + c % 2, 0:D], hT[:, k, c * P:c * P + n], w2s[:, h, k, :],
                                         start=(k == 0), stop=(k == KF - 1))
                    last.then_inc(y_psum, 1)

            tokens(0, 0)
            mm_expert(0, 0)
            mm_expert(1, 1)
            with pe.Fori(2, X - 3, 2) as e:
                mm_expert(e, 0)
                mm_expert(e + 1, 1)
            mm_expert(X - 2, 0)
            mm_expert(X - 1, 1, more=False)
            pe.wait_ge(fin_dve, 1)
            pe.matmul(PS[:, TP, 0:1], ones[:, :], yfin[:, :], start=True, stop=True).then_inc(fin_pe, 1)


_INS = ["x", "src", "dst", "edge_type_8", "L0_gnn_W_rel", "L0_gnn_W_root", "L0_gnn_bias", "L0_ffn_gate_w",
        "L0_ffn_gate_b", "L0_ffn_w1", "L0_ffn_b1", "L0_ffn_w2", "L0_ffn_b2"]


def kernel(**inputs):
    import concourse.bacc as bacc
    from concourse.bass_utils import run_bass_kernel_spmd

    nc = bacc.Bacc("TRN2", target_bir_lowering=False, num_devices=1)
    arrays, args = {}, []
    for name in _INS:
        a = np.ascontiguousarray(inputs[name])
        arrays[f"in_{name}"] = a
        args.append(nc.dram_tensor(f"in_{name}", a.shape, mybir.dt.from_np(a.dtype), kind="ExternalInput").ap())
    args.append(nc.dram_tensor("out", (N, D), F32, kind="ExternalOutput").ap())
    ffn_gnn(nc, *args)
    r = run_bass_kernel_spmd(nc, [arrays], core_ids=[0])
    return r.results[0]["out"]
```
